# Optimizing a Trainium2 kernel written in Bass

```python
import numpy as np
import jax
import jax.numpy as jnp

def _softmax(x, axis=-1):
    return jax.nn.softmax(x, axis=axis)

def _gelu(x):
    return jax.nn.gelu(x, approximate=True)

def _silu(x):
    return jax.nn.silu(x)

def _sigmoid(x):
    return jax.nn.sigmoid(x)

def _layernorm(x, axis=-1, eps=1e-05):
    m = jnp.mean(x, axis=axis, keepdims=True)
    v = jnp.var(x, axis=axis, keepdims=True)
    return (x - m) / jnp.sqrt(v + eps)

def _scatter_add(tgt, idx, src, axis=0):
    return tgt.at[idx].add(src)

def _segment_sum(src, seg, n):
    return jax.ops.segment_sum(src, seg, n)
kernel_name = 'mk_audio_tower_d1_tok_audfeat1024_r4_a05583'

def setup_inputs(seed: int=0):
    np.random.seed(seed)
    _w = jnp.asarray

    def _rec_inputs():
        import jax
        import jax.numpy as jnp
        _rk = jax.random.key(seed)
        x = -0.000125008 + 0.999885 * jax.random.normal(jax.random.fold_in(_rk, 1), (64, 125, 128), jnp.float32)
        return x
    x = _rec_inputs()

    def _L0_tok_setup():
        import jax, jax.numpy as jnp
        import numpy as np
        PT, PF = (16, 16)
        EPS = 1e-06
        key = jax.random.key(seed)
        k1, k2, k3 = jax.random.split(key, 3)
        B, T, F = (64, 1024, 128)
        E = 256
        patch_dim = PT * PF
        x = jax.random.normal(k1, (B, T, F), dtype=jnp.float32)
        W = jax.random.normal(k2, (patch_dim, E), dtype=jnp.float32) * (1.0 / np.sqrt(patch_dim))
        b = jax.random.normal(k3, (E,), dtype=jnp.float32) * 0.02
        gamma = jnp.ones((E,), dtype=jnp.float32)
        beta = jnp.zeros((E,), dtype=jnp.float32)
        return {'x': x, 'W': W, 'b': b, 'gamma': gamma, 'beta': beta}
    _L0_tok_all = _L0_tok_setup()
    _L0_tok_in = {k: v for k, v in _L0_tok_all.items() if k in ('W', 'b', 'gamma', 'beta')}
    del _L0_tok_all

    def _L0_attn_setup():
        import jax, jax.numpy as jnp
        import numpy as np
        B, N, DM, H = (1, 512, 256, 16)
        CURV = 1.0
        key = jax.random.key(seed)
        ks = jax.random.split(key, 5)
        s = 1.0 / np.sqrt(DM)
        x = jax.random.normal(ks[0], (B, N, DM), dtype=jnp.float32)
        Wq = jax.random.uniform(ks[1], (DM, DM), jnp.float32, -s, s)
        Wk = jax.random.uniform(ks[2], (DM, DM), jnp.float32, -s, s)
        Wv = jax.random.uniform(ks[3], (DM, DM), jnp.float32, -s, s)
        Wo = jax.random.uniform(ks[4], (DM, DM), jnp.float32, -s, s)
        return {'x': x, 'Wq': Wq, 'Wk': Wk, 'Wv': Wv, 'Wo': Wo}
    _L0_attn_all = _L0_attn_setup()
    _L0_attn_in = {k: v for k, v in _L0_attn_all.items() if k in ('Wq', 'Wk', 'Wv', 'Wo')}
    del _L0_attn_all

    def _L0_ffn_setup():
        import jax, jax.numpy as jnp
        import numpy as np
        B, S, D, F, E, K = (4, 512, 256, 1024, 4, 2)
        key = jax.random.key(seed)
        k = jax.random.split(key, 6)
        x = jax.random.normal(k[0], (B, S, D), jnp.float32)
        router_w = jax.random.normal(k[1], (D, E), jnp.float32) * D ** (-0.5)
        router_b = jnp.zeros((E,), jnp.float32)
        w1 = jax.random.normal(k[2], (E, D, F), jnp.float32) * 0.02
        w3 = jax.random.normal(k[3], (E, D, F), jnp.float32) * 0.02
        w2 = jax.random.normal(k[4], (E, F, D), jnp.float32) * 0.02
        return {'x': x, 'router_w': router_w, 'router_b': router_b, 'w1': w1, 'w3': w3, 'w2': w2}
    _L0_ffn_all = _L0_ffn_setup()
    _L0_ffn_in = {k: v for k, v in _L0_ffn_all.items() if k in ('router_w', 'router_b', 'w1', 'w3', 'w2')}
    del _L0_ffn_all
    return {'x': x, 'L0_tok_W': _L0_tok_in['W'], 'L0_tok_b': _L0_tok_in['b'], 'L0_tok_gamma': _L0_tok_in['gamma'], 'L0_tok_beta': _L0_tok_in['beta'], 'L0_attn_Wq': _L0_attn_in['Wq'], 'L0_attn_Wk': _L0_attn_in['Wk'], 'L0_attn_Wv': _L0_attn_in['Wv'], 'L0_attn_Wo': _L0_attn_in['Wo'], 'L0_ffn_router_w': _L0_ffn_in['router_w'], 'L0_ffn_router_b': _L0_ffn_in['router_b'], 'L0_ffn_w1': _L0_ffn_in['w1'], 'L0_ffn_w3': _L0_ffn_in['w3'], 'L0_ffn_w2': _L0_ffn_in['w2']}

def reference(x, L0_tok_W, L0_tok_b, L0_tok_gamma, L0_tok_beta, L0_attn_Wq, L0_attn_Wk, L0_attn_Wv, L0_attn_Wo, L0_ffn_router_w, L0_ffn_router_b, L0_ffn_w1, L0_ffn_w3, L0_ffn_w2):
    import jax
    import jax.numpy as jnp

    def _L0_tok_ref(x, W, b, gamma, beta):
        import jax, jax.numpy as jnp
        import numpy as np
        PT, PF = (16, 16)
        EPS = 1e-06
        B, T, F = x.shape
        pad_f = -F % PF
        pad_t = -T % PT
        if pad_f or pad_t:
            x = jnp.pad(x, ((0, 0), (0, pad_t), (0, pad_f)))
            T, F = (T + pad_t, F + pad_f)
        nt, nf = (T // PT, F // PF)
        p = x.reshape(B, nt, PT, nf, PF).transpose(0, 1, 3, 2, 4).reshape(B, nt * nf, PT * PF)
        y = jnp.einsum('bpd,de->bpe', p, W) + b
        mu = jnp.mean(y, axis=-1, keepdims=True)
        var = jnp.mean(jnp.square(y - mu), axis=-1, keepdims=True)
        y = (y - mu) * jax.lax.rsqrt(var + EPS) * gamma + beta
        return y

    def _L0_attn_ref(x, Wq, Wk, Wv, Wo):
        import jax, jax.numpy as jnp
        import numpy as np
        B, N, DM, H = (1, 512, 256, 16)
        CURV = 1.0
        b, n, d = x.shape
        hd = d // H

        def split_heads(t):
            return t.reshape(b, n, H, hd).transpose(0, 2, 1, 3)
        q = split_heads(x @ Wq.T)
        k = split_heads(x @ Wk.T)
        v = split_heads(x @ Wv.T)
        q_norm_sq = jnp.sum(q * q, axis=-1, keepdims=True)
        k_norm_sq = jnp.sum(k * k, axis=-1)[:, :, None, :]
        qk = jnp.einsum('bhnd,bhmd->bhnm', q, k)
        diff_sq = jnp.maximum(q_norm_sq + k_norm_sq - 2.0 * qk, 0.0)
        denom = jnp.maximum((1.0 - CURV * q_norm_sq) * (1.0 - CURV * k_norm_sq), 1e-06)
        cosh_arg = jnp.maximum(1.0 + 2.0 * CURV * diff_sq / denom, 1.0)
        distance = jnp.where(cosh_arg > 1.0, jnp.arccosh(jnp.maximum(cosh_arg, 1.0 + 1e-12)), 0.0)
        attn = jax.nn.softmax(-distance, axis=-1)
        out = jnp.einsum('bhnm,bhmd->bhnd', attn, v)
        out = out.transpose(0, 2, 1, 3).reshape(b, n, d)
        return out @ Wo.T

    def _L0_ffn_ref(x, router_w, router_b, w1, w3, w2):
        import jax, jax.numpy as jnp
        import numpy as np
        B, S, D, F, E, K = (4, 512, 256, 1024, 4, 2)
        b, s, d = x.shape
        T = b * s
        e = router_w.shape[1]
        xf = x.reshape(T, d)
        logits = xf @ router_w + router_b
        probs = jax.nn.softmax(logits, axis=-1)
        top_p, top_i = jax.lax.top_k(probs, K)
        top_p = top_p / jnp.sum(top_p, axis=-1, keepdims=True)
        gates = jnp.zeros((T, e), xf.dtype).at[jnp.arange(T)[:, None], top_i].add(top_p)
        h = jax.nn.silu(jnp.einsum('td,edf->etf', xf, w1)) * jnp.einsum('td,edf->etf', xf, w3)
        expert_out = jnp.einsum('etf,efd->etd', h, w2)
        out = jnp.einsum('te,etd->td', gates, expert_out)
        return out.reshape(b, s, d)
    h = _L0_tok_ref(x, L0_tok_W, L0_tok_b, L0_tok_gamma, L0_tok_beta)
    h = h + _L0_attn_ref(_layernorm(h, axis=-1), L0_attn_Wq, L0_attn_Wk, L0_attn_Wv, L0_attn_Wo)
    h = h + _L0_ffn_ref(_layernorm(h, axis=-1), L0_ffn_router_w, L0_ffn_router_b, L0_ffn_w1, L0_ffn_w3, L0_ffn_w2)
    return h

_drawn_inputs = setup_inputs


def setup_inputs(seed=0):
    import zlib

    import numpy as np

    out = dict(_drawn_inputs(seed))
    spreads = {'L0_tok_gamma': (1.0, 0.2), 'L0_tok_beta': (0.0, 0.1), 'L0_ffn_router_b': (0.0, 0.8)}
    factors = {'L0_attn_Wq': 7.743, 'L0_attn_Wk': 5.737, 'L0_ffn_router_w': 2.949}
    for name, (base, spread) in spreads.items():
        noise = np.random.default_rng([zlib.crc32(name.encode()), seed]).standard_normal(out[name].shape)
        drawn = base * np.exp(spread * noise) if base else spread * noise
        out[name] = jnp.asarray(drawn.astype(out[name].dtype))
    for name, factor in factors.items():
        out[name] = (out[name] * factor).astype(out[name].dtype)
    return out
```

```python
from contextlib import ExitStack

import concourse.bass as bass
from concourse import mybir

F32 = mybir.dt.float32
F32R = mybir.dt.float32r
I32 = mybir.dt.int32
U32 = mybir.dt.uint32
ALU = mybir.AluOpType
ACT = mybir.ActivationFunctionType
AX = mybir.AxisListType

CLIPS, SEQ, HEADS, HD = 64, 64, 16, 16
DM = HEADS * HD
TOKENS = CLIPS * SEQ
TILE = 128
PAIRS = TOKENS // (2 * TILE)
EXPERTS, FF = 4, 1024
KC = DM // 128
R = 32
VW = HD + 1
BLOCK = 512
REGION = TOKENS + BLOCK
BLOCKS = (2 * TOKENS + EXPERTS * (BLOCK - 1)) // BLOCK
ROW = 264
FCH = FF // 128
BASED, SLOTTED = 6, 14
EARLY = 2

C = {}
_at = 0
for _name, _width in (("ident", 128), ("fold", 64), ("tri", 128), ("ones", 128), ("clip", 2), ("negclip", 2),
                      ("head", 16), ("after", 16), ("before", 16), ("region", 4), ("steps", 9), ("number", 2),
                      ("blockno", BLOCKS), ("eps_tok", 1), ("eps_ln", 1), ("one", 1), ("dump", 4)):
    C[_name] = (_at, _at + _width)
    _at += _width
NCONST = _at


def constants():
    import numpy as np

    c = np.zeros((128, NCONST), np.float32)
    p = np.arange(128)

    def put(name, value):
        c[:, C[name][0]:C[name][1]] = value

    put("ident", np.eye(128))
    put("fold", p[:, None] % 64 == np.arange(64))
    put("tri", p[:, None] < p)
    put("ones", 1)
    clip = (p[:, None] // 64 == np.arange(2)).astype(np.float32)
    put("clip", clip)
    put("negclip", -clip)
    put("head", p[:, None] % 16 == np.arange(16))
    i, j = np.arange(16) // 4, np.arange(16) % 4
    put("after", j > i)
    put("before", j < i)
    put("region", np.arange(EXPERTS) * REGION)
    put("steps", np.arange(9) * BLOCK)
    put("number", p[:, None] + np.arange(2) * 128)
    put("blockno", np.arange(BLOCKS))
    put("eps_tok", 1e-6)
    put("eps_ln", 1e-5)
    put("one", 1)
    put("dump", TOKENS + p[:, None] + 128 * np.arange(4))
    return c


def wait(eng, sem, value):
    if not isinstance(value, int) or value > 0:
        eng.wait_ge(sem, value)


def wait_apart(eng, passed, sem, value):
    wait(eng, sem, value)
    eng.sem_inc(passed, 1)


def walk(eng, step):
    first, last = 4, PAIRS - 3
    for i in range(-1, first):
        step(i, i % 2, i + 1 < PAIRS, 0 <= i, 1 <= i, 2 <= i)
    with eng.Fori(0, (last - first + 1) // 2) as n:
        for s in range(2):
            step(2 * n + first + s, (first + s) % 2, True, True, True, True)
    for i in range(last + 1, PAIRS + 2):
        step(i, i % 2, i + 1 < PAIRS, i < PAIRS, i < PAIRS + 1, True)


class Shared:

    def __init__(self, nc, ctx):
        def sb(name, shape, dt=F32):
            return ctx.enter_context(nc.sbuf_tensor(name, shape, dt))

        self.chosen = sb("chosen", [128, BLOCKS, EXPERTS])
        self.table = sb("table", [1, 2 * BLOCKS], I32)
        self.xg = sb("xg", [128, 4, ROW])
        self.wa = sb("wa", [128, FCH, 2, KC, 128])
        self.wb = sb("wb", [128, FCH, DM])
        self.scat_hi = ctx.enter_context(nc.semaphore("scat_hi"))
        self.scat_lo = ctx.enter_context(nc.semaphore("scat_lo"))
        self.x_in = ctx.enter_context(nc.semaphore("x_in"))
        self.wa_in = [ctx.enter_context(nc.semaphore(f"wa_in{c}")) for c in range(FCH)]
        self.wb_in = [ctx.enter_context(nc.semaphore(f"wb_in{c}")) for c in range(FCH)]

    def load_rows(self, sp, rows, i):
        r = sp.value_load(self.table[0:1, bass.ds(i + BLOCKS, 1)], min_val=0, max_val=EXPERTS * REGION)
        sp.dma_start(self.xg[:, :, :], rows[bass.ds(r, BLOCK), :].rearrange("(s p) n -> p s n", p=128))\
          .then_inc(self.x_in, 16)

    def expert(self, sp, i):
        return sp.value_load(self.table[0:1, bass.ds(i, 1)], min_val=0, max_val=EXPERTS - 1)

    def load_wa(self, sp, w13, e, c):
        sp.dma_start(self.wa[:, c, :, :, :].rearrange("p b c d -> p (b c d)"), w13[e, c]).then_inc(self.wa_in[c], 16)

    def load_wb(self, sp, w2, e, c):
        sp.dma_start(self.wb[:, c, :], w2[e, c]).then_inc(self.wb_in[c], 16)


def attention_phase(nc, patches, w_tok, vecs, w_qkv, w_o, w_r, consts, w13, w2, out, rows, shared):
    with ExitStack() as ctx:
        def sb(name, shape, dt=F32):
            return ctx.enter_context(nc.sbuf_tensor(name, shape, dt))

        def sem(name):
            return ctx.enter_context(nc.semaphore(name))

        K = sb("K", [128, NCONST])
        wtok = sb("wtok", [128, KC, DM])
        wqkv = sb("wqkv", [128, KC, 3 * DM])
        wo = sb("wo", [128, 2, DM])
        wr = sb("wr", [128, KC, EXPERTS])
        vec = sb("vec", [128, 3, DM])
        rbias = sb("rbias", [128, EXPERTS])

        def k(name):
            return K[:, C[name][0]:C[name][1]]

        pt = sb("pt", [128, 2, KC, 128])
        y = sb("y", [128, 2, DM])
        yg = sb("yg", [128, 2, DM])
        st1 = sb("st1", [128, 2, 6])
        mv1 = sb("mv1", [128, 2, 2])
        sd1 = sb("sd1", [128, 2])
        rs1 = sb("rs1", [128, 2])
        st2 = sb("st2", [128, 2, 6])
        mv2 = sb("mv2", [128, 2, 2])
        sd2 = sb("sd2", [128, 2])
        rs2 = sb("rs2", [128, 2])
        h = [sb(f"h{s}", [128, 2, DM]) for s in range(2)]
        held = sb("held", [128, 2, DM])
        hn = sb("hn", [128, 2, DM])
        hnT = sb("hnT", [128, 2, KC, 128])
        sq = sb("sq", [128, 2, 2 * DM])
        nrm = sb("nrm", [128, 2, 2, HEADS])
        aug = sb("aug", [128, 2, 2, HEADS, 2, R])
        xb = sb("xb", [128, 2, 2, 2, HEADS])
        yb = sb("yb", [128, 2, 2, HEADS])
        v = [sb(f"v{s}", [128, 2, 8, 2, 2, VW]) for s in range(2)]
        tk = sb("tk", [128, 2, 8, 128])
        tq = sb("tq", [128, 2, 8, 2, 64])
        xT = sb("xT", [64, 2, 128])
        ybd = sb("ybd", [64, HEADS * 64])
        dist = sb("dist", [128, 2, 1024])
        den = sb("den", [128, 2, 1024])
        dsum = sb("dsum", [128, 2, 1024])
        prob = sb("prob", [128, 2, 1024])
        rden = sb("rden", [128, 2, 2, 4, 2])
        an = sb("an", [128, 2, 2, 8, HD])
        at = sb("at", [128, 2, 2, 2, 64])
        x2 = sb("x2", [128, 2, DM])
        st3 = sb("st3", [128, 2, 6])
        mv3 = sb("mv3", [128, 2, 2])
        sd3 = sb("sd3", [128, 2])
        rs3 = sb("rs3", [128, 2])
        xrow = [sb(f"xrow{s}", [128, 2, ROW]) for s in range(2)]
        xnT = sb("xnT", [128, 2, KC, 128])
        lg = sb("lg", [128, 2, 4])
        gt = sb("gt", [128, 2, 4, 4])
        ge = sb("ge", [128, 2, 4, 4])
        rk2 = sb("rk2", [128, 2, 4, 2])
        rk = sb("rk", [128, 2, 4])
        mask = [sb(f"mask{s}", [128, 2, 4]) for s in range(2)]
        m2 = sb("m2", [128, 2, 2])
        m1 = sb("m1", [128, 2, 1])
        lm = sb("lm", [128, 2, 4])
        ex = sb("ex", [128, 2, 4])
        s1 = sb("s1", [128, 2])
        r1 = sb("r1", [128, 2])
        pr = sb("pr", [128, 2, 4])
        mg = sb("mg", [128, 2, 4])
        s2 = sb("s2", [128, 2])
        r2 = sb("r2", [128, 2])
        tokno = sb("tokno", [128, 2])
        px = sb("px", [128, 2, 2, 4])
        base = sb("base", [128, 4])
        mid = sb("mid", [128, 4])
        slot = sb("slot", [128, 2, 4])
        t2 = sb("t2", [128, 2, 2])
        hi = sb("hi", [128, 2, 1])
        t3 = sb("t3", [128, 2, 3])
        lo = sb("lo", [128, 2, 1])
        tot = sb("tot", [128, 2, 1])
        ihi = sb("ihi", [128, 2, 1], U32)
        ilo = sb("ilo", [128, 2, 1], U32)
        pad = sb("pad", [128, 4, ROW])
        cnt = sb("cnt", [128, 4])
        cmpb = sb("cmpb", [128, 4, 9])
        nb = sb("nb", [128, 4])
        cum = sb("cum", [128, 4])
        past = sb("past", [128, 4, BLOCKS])
        be = sb("be", [128, BLOCKS])
        bs = sb("bs", [128, 3, BLOCKS])
        brow = sb("brow", [128, BLOCKS])
        bt1 = sb("bt1", [128, BLOCKS])
        bt2 = sb("bt2", [128, BLOCKS])
        tabf = sb("tabf", [128, 2 * BLOCKS])
        padrow = sb("padrow", [1, EXPERTS], I32)
        chosen = shared.chosen

        PS = ctx.enter_context(nc.psum_tensor("PS", [128, 8, 512], F32))
        M0, M1, M2, M3, P0, D0, D1, P1 = (PS[:, n, :] for n in range(8))
        DB, PB = (D0, D1), (P0, P1)

        names = """const_in pt_in e_done y_ready st1_ready mv1_ready sd1_ready rs1_ready yg_ready h_ready held_in
            st2_ready mv2_ready sd2_ready rs2_ready hn_ready ht_done hnT_ready qk_done v_done sq_ready data_ready
            v_ready nrm_ready nq_ready aug_ready tk_done tka_ready tkb_ready tq_done tq_ready xy_done xt_ready ybd_ready
            d_done p_done dist_ready den_ready dsum_ready ra_ready rb_ready c_ready ln_ready e_ready w_ready
            av_done rden_ready an_ready at_done at_ready wo_done x2_ready st3_ready mv3_ready sd3_ready rs3_ready
            xn_ready xnt_done xnT_ready lg_done lg_ready gt_ready ge_ready rk_ready mask_ready lm_ready ex_ready
            px_done px_ready gate_step gate_ready tok_step slot_step slot_ready out_stored
            zero_ready padzero_ready init_ready tab_step pad_ready padrow_ready tab_ready pad_out embed_in passed_pe passed_dve passed_pool""".split()
        S = {n: sem(n) for n in names}
        S["scat_hi"], S["scat_lo"] = shared.scat_hi, shared.scat_lo
        block = ctx.enter_context(nc.Block())

        @block.sync
        def _(sp):
            for dst, src, ready in ((K[:, :], consts, "embed_in"), (wtok[:, :, :], w_tok, "embed_in"),
                                    (vec[:, :, :], vecs[:, 0:3 * DM].rearrange("p (a n) -> p a n", a=3), "embed_in"),
                                    (rbias[:, :], vecs[:, 3 * DM:3 * DM + 4], "const_in"), (wqkv[:, :, :], w_qkv, "const_in"),
                                    (wo[:, :, :], w_o, "const_in"), (wr[:, :, :], w_r, "const_in")):
                if ready == "const_in" and src is w_qkv:
                    sp.dma_start(pt[:, :, :, :], patches[0]).then_inc(S["pt_in"], 16)
                sp.dma_start(dst, src).then_inc(S[ready], 16)

            def write_padding():
                sp.wait_ge(S["pad_ready"], 1)
                sp.wait_ge(S["padrow_ready"], 1)
                for e in range(EXPERTS):
                    end = sp.value_load(padrow[0:1, e:e + 1], min_val=e * REGION, max_val=e * REGION + TOKENS - 2 * TILE)
                    for at, tiles in ((0, 4), (BLOCK, 2)):
                        sp.dma_start(rows[bass.ds(end + at, tiles * 128), :].rearrange("(s p) n -> p s n", p=128),
                                     pad[:, 0:tiles, :]).then_inc(S["pad_out"], 16)
                sp.dma_start(rows[EXPERTS * REGION:EXPERTS * REGION + BLOCK, :].rearrange("(s p) n -> p s n", p=128),
                             pad[:, :, :]).then_inc(S["pad_out"], 16)

            def step(i, par, front, att, back, route):
                if isinstance(i, int) and i == PAIRS:
                    write_padding()
                if front and not (isinstance(i, int) and i < 0):
                    wait(sp, S["e_done"], i + 1)
                    sp.dma_start(pt[:, :, :, :], patches[i + 1]).then_inc(S["pt_in"], 16)
                if back:
                    wait(sp, S["x2_ready"], i)
                    sp.dma_start(out[bass.ds((i - 1) * 256, 256), :].rearrange("(u p) n -> p u n", p=128),
                                 x2[:, :, :]).then_inc(S["out_stored"], 16)
                if att:
                    wait(sp, S["h_ready"], 2 * i + 2)
                    sp.dma_start(held[:, :, :], h[par][:, :, :]).then_inc(S["held_in"], 16)
            walk(sp, step)
            sp.wait_ge(S["tab_ready"], 1)
            e = shared.expert(sp, 0)
            for c in range(EARLY):
                shared.load_wa(sp, w13, e, c)
            sp.wait_ge(S["out_stored"], 16 * PAIRS)

        @block.tensor
        def _(pe):
            pe.wait_ge(S["embed_in"], 16 * 3)

            def distances(a, u):
                if u == 1:
                    wait(pe, S["dist_ready"], 4 * a + 2)
                for j in range(8):
                    mm = pe.matmul(DB[j // 4][:, (j % 4) * 128:(j % 4 + 1) * 128], tk[:, u, j, :],
                                   tq[:, u, j, :, :].rearrange("p g q -> p (g q)"), start=True, stop=True)
                mm.then_inc(S["d_done"], 1)

            def densities(a, u, g):
                if u == 1:
                    wait(pe, S["den_ready"], 4 * a + 2 - g)
                pe.matmul(PB[g][:, :], xT[:, u, :], ybd[:, g * 512:(g + 1) * 512],
                          start=True, stop=True).then_inc(S["p_done"], 1)

            def project(u):
                for c in range(KC):
                    mm = pe.matmul(PS[:, 2 * u, :], hnT[:, u, c, :], wqkv[:, c, 0:2 * DM],
                                   start=(c == 0), stop=(c == KC - 1))
                mm.then_inc(S["qk_done"], 1)
                for c in range(KC):
                    mm = pe.matmul(PS[:, 2 * u + 1, 0:DM], hnT[:, u, c, :], wqkv[:, c, 2 * DM:3 * DM],
                                   start=(c == 0), stop=(c == KC - 1))
                mm.then_inc(S["v_done"], 1)

            def step(i, par, front, att, back, route):
                f, a, b = i + 1, i, i - 1
                if front:
                    wait(pe, S["pt_in"], 16 * (f + 1))
                    wait(pe, S["tka_ready"], 2 * f - 1)
                    for u in range(2):
                        for c in range(KC):
                            mm = pe.matmul(M0[:, u * DM:(u + 1) * DM], pt[:, u, c, :], wtok[:, c, :],
                                           start=(c == 0), stop=(c == KC - 1))
                    mm.then_inc(S["e_done"], 1)
                if att or back:
                    wait(pe, S["tka_ready"], 2 * (i + 1) if att else 2 * PAIRS)
                    wait(pe, S["tkb_ready"], 2 * (i + 1) if att else 2 * PAIRS)
                if back:
                    wait(pe, S["v_ready"], 4 * i)
                    for u in range(2):
                        wait(pe, S["w_ready"], 2 * b + u + 1)
                        if u == 1:
                            wait(pe, S["xt_ready"], i + 1 if att else PAIRS)
                            wait(pe, S["ybd_ready"], i + 1 if att else PAIRS)
                        for j in range(8):
                            bank = PS[:, 1 + 2 * u + j // 4, (j % 4) * 4 * VW:(j % 4 + 1) * 4 * VW]
                            mm = pe.matmul(bank, prob[:, u, j * 128:(j + 1) * 128],
                                           v[1 - par][:, u, j, :, :, :].rearrange("p a b c -> p (a b c)"),
                                           start=True, stop=True)
                        mm.then_inc(S["av_done"], 1)
                if att:
                    wait(pe, S["tq_ready"], 4 * a + 4)
                    distances(a, 0)
                    wait(pe, S["xt_ready"], a + 1)
                    wait(pe, S["ybd_ready"], a + 1)
                    wait(pe, S["px_ready"], i - 1)
                    densities(a, 0, 1)
                if back:
                    wait(pe, S["an_ready"], 8 * i)
                    for u in range(2):
                        for c in range(2):
                            mm = pe.transpose(M1[:, (2 * u + c) * 128:(2 * u + c + 1) * 128],
                                              an[:, u, c, :, :].rearrange("p a b -> p (a b)"), k("ident"))
                    mm.then_inc(S["at_done"], 1)
                if att:
                    densities(a, 0, 0)
                if back:
                    wait(pe, S["at_ready"], 2 * i)
                    for u in range(2):
                        for g in range(2):
                            mm = pe.matmul(M2[:, u * DM:(u + 1) * DM], at[:, u, g, :, :].rearrange("p c q -> p (c q)"), wo[:, g, :],
                                           start=(g == 0), stop=(g == 1))
                    mm.then_inc(S["wo_done"], 1)
                if att:
                    distances(a, 1)
                if front:
                    wait(pe, S["hn_ready"], 2 * f + 2)
                    for u in range(2):
                        for c in range(KC):
                            mm = pe.transpose(M3[:, (2 * u + c) * 128:(2 * u + c + 1) * 128],
                                              hn[:, u, c * 128:(c + 1) * 128], k("ident"))
                    mm.then_inc(S["ht_done"], 1)
                if att:
                    densities(a, 1, 1)
                    densities(a, 1, 0)
                if front:
                    wait(pe, S["hnT_ready"], f + 1)
                    if isinstance(i, int) and i < 0:
                        pe.wait_ge(S["const_in"], 16 * 4)
                        pe.wait_ge(S["init_ready"], 6)
                    if back:
                        wait(pe, S["x2_ready"], i)
                    project(0)
                if back:
                    wait(pe, S["xn_ready"], 2 * i)
                    if att:
                        wait(pe, S["den_ready"], 4 * a + 4)
                    for u in range(2):
                        for c in range(KC):
                            mm = pe.transpose(P1[:, (2 * u + c) * 128:(2 * u + c + 1) * 128],
                                              xrow[1 - par][:, u, c * 128:(c + 1) * 128], k("ident"))
                    mm.then_inc(S["xnt_done"], 1)
                if front:
                    project(1)
                if back:
                    wait(pe, S["xnT_ready"], i)
                    for u in range(2):
                        for c in range(KC):
                            mm = pe.matmul(P1[:, u * 4:u * 4 + 4], xnT[:, u, c, :], wr[:, c, :],
                                           start=(c == 0), stop=(c == KC - 1))
                    mm.then_inc(S["lg_done"], 1)
                if front:
                    for u in range(2):
                        wait(pe, S["aug_ready"], 4 * (2 * f + u + 1))
                        wait(pe, S["data_ready"], 2 * (2 * f + u + 1))
                        wait(pe, S["sq_ready"], 2 * f + u + 1)
                        wait(pe, S["v_ready"], 4 * f + 2 * u + 2)
                        for m in range(8):
                            mm = pe.transpose(PS[:, 2 * u + m // 4, (m % 4) * 128:(m % 4 + 1) * 128],
                                              aug[:, u, 1, 2 * m:2 * m + 2, :, :].rearrange("p a b c -> p (a b c)"),
                                              k("ident"))
                        mm.then_inc(S["tk_done"], 1)
                        if att:
                            wait(pe, S["dist_ready"], 4 * a + 3 + u)
                        for m in range(8):
                            mm = pe.matmul(DB[u][:, m * 64:(m + 1) * 64],
                                           aug[:, u, 0, 2 * m:2 * m + 2, :, :].rearrange("p a b c -> p (a b c)"),
                                           k("fold"), start=True, stop=True)
                        mm.then_inc(S["tq_done"], 1)
                    wait_apart(pe, S["passed_pe"], S["den_ready"], 4 * a + 4 if att else 0)
                    for u in range(2):
                        pe.transpose(P0[0:64, u * 128:(u + 1) * 128], xb[:, u, :, :, :].rearrange("p a b c -> p (a b c)"),
                                     k("ident"))
                        mm = pe.matmul(P0[32 * u:32 * u + 32, 256:320], yb[:, u, :, :].rearrange("p a b -> p (a b)"),
                                       k("fold"), start=True, stop=True)
                    mm.then_inc(S["xy_done"], 1)
                if back:
                    wait(pe, S["mask_ready"], i)
                    wait(pe, S["lg_ready"], i)
                    msk = mask[1 - par][:, :, :].rearrange("p a b -> p (a b)")
                    pe.matmul(P1[:, 16:24], k("tri"), msk, start=True, stop=True)
                    pe.matmul(P1[:, 24:32], k("ones"), msk, start=True, stop=True).then_inc(S["px_done"], 1)
            walk(pe, step)

        @block.vector
        def _(dve):
            dve.memset(aug[:, :, :, :, :, :], 0.0).then_inc(S["zero_ready"], 1)
            for s in range(2):
                dve.memset(v[s][:, :, :, :, :, :], 0.0).then_inc(S["zero_ready"], 1)
            dve.memset(tq[:, :, :, :, :], 0.0).then_inc(S["zero_ready"], 1)
            dve.memset(xb[:, :, :, :, :], 0.0).then_inc(S["init_ready"], 1)
            dve.wait_ge(S["zero_ready"], 4)
            for c in range(2):
                for u in range(2):
                    own = slice(64 * c, 64 * c + 64)
                    dve.memset(aug[own, u, 0, :, c, HD + 1:HD + 2], 1.0)
                    dve.memset(aug[own, u, 1, :, c, HD:HD + 1], 1.0)
                    for s in range(2):
                        last = dve.memset(v[s][own, u, :, c, :, HD:VW], 1.0)
                last.then_inc(S["init_ready"], 1)
            dve.wait_ge(S["embed_in"], 16 * 3)
            dve.tensor_copy(base[:, :], k("region")).then_inc(S["init_ready"], 1)
            dve.tensor_copy(tokno[:, :], k("number")).then_inc(S["init_ready"], 1)

            def stats(src, st, mv, p, n1, n2, ready, upto):
                dve.wait_ge(ready, upto)
                for u in range(2):
                    last = dve.bn_stats(st[:, u, :], src(u)).then_inc(S[n1], 1)
                wait_apart(dve, S["passed_dve"], S[n1], 2 * p + 2)
                for u in range(2):
                    last = dve.bn_aggr(mv[:, u, :], st[:, u, :]).then_inc(S[n2], 1)

            def inverse(sd, rs, p, n1, n2):
                dve.wait_ge(S[n1], p + 1)
                dve.reciprocal(rs[:, :], sd[:, :]).then_inc(S[n2], 1)
                dve.wait_ge(S[n2], p + 1)

            def densities(a, u):
                for half in (1, 0):
                    dve.wait_ge(S["p_done"], 4 * a + 2 * u + 2 - half)
                    if u == 0 and half == 1:
                        wait(dve, S["w_ready"], 2 * a)
                    dve.tensor_scalar(den[:, u, half * 512:(half + 1) * 512], PB[half][:, :], 1e-6, None,
                                      ALU.max).then_inc(S["den_ready"], 1)

            def add_density(a, u):
                dve.wait_ge(S["dist_ready"], 4 * a + 2 * u + 2)
                dve.wait_ge(S["den_ready"], 4 * a + 2 * u + 2)
                dve.tensor_tensor(dsum[:, u, :], dist[:, u, :], den[:, u, :], ALU.add).then_inc(S["dsum_ready"], 1)

            def probabilities(a, u):
                dve.wait_ge(S["e_ready"], 2 * a + u + 1)
                if u == 0:
                    wait(dve, S["av_done"], 2 * a)
                dve.tensor_tensor(prob[:, u, :], dist[:, u, :], den[:, u, :], ALU.mult).then_inc(S["w_ready"], 1)

            def normalise(b, u):
                dve.wait_ge(S["av_done"], 2 * b + u + 1)
                for g in range(2):
                    own = slice(64 * g, 64 * g + 64)
                    den_ps = PS[own, 1 + 2 * u:3 + 2 * u, 0:16 * VW].rearrange(
                        "p k (j c d e) -> p k j c d e", j=4, c=2, d=2)[:, :, :, :, g, HD]
                    dve.reciprocal(rden[own, u, :, :, :], den_ps).then_inc(S["rden_ready"], 1)
                if u == 0:
                    wait(dve, S["at_done"], b)
                for g in range(2):
                    own = slice(64 * g, 64 * g + 64)
                    dve.wait_ge(S["rden_ready"], 4 * b + 2 * u + g + 1)
                    for q in range(2):
                        o_ps = PS[own, 1 + 2 * u + q, 0:16 * VW].rearrange(
                            "p (j c d e) -> p j c d e", j=4, c=2, d=2)[:, :, :, g, 0:HD]
                        dst = an[own, u, :, 4 * q:4 * q + 4, :].rearrange("p c j e -> p j c e")
                        dve.tensor_tensor(dst, o_ps, rden[own, u, q, :, :].unsqueeze(3).to_broadcast([64, 4, 2, HD]),
                                          ALU.mult).then_inc(S["an_ready"], 1)

            def gates(c, par):
                g0 = 5 * c
                dve.wait_ge(S["ex_ready"], c + 1)
                dve.tensor_tensor(mg[:, :, :], ex[:, :, :], mask[par][:, :, :], ALU.mult).then_inc(S["gate_step"], 1)
                dve.wait_ge(S["gate_step"], g0 + 1)
                dve.tensor_reduce(s2[:, :], mg[:, :, :], AX.X, ALU.add).then_inc(S["gate_step"], 1)
                dve.wait_ge(S["gate_step"], g0 + 2)
                dve.reciprocal(r2[:, :], s2[:, :]).then_inc(S["gate_step"], 1)
                dve.wait_ge(S["gate_step"], g0 + 3)
                dve.tensor_tensor(xrow[par][:, :, DM:DM + 4], mg[:, :, :],
                                  r2[:, :].unsqueeze(2).to_broadcast([128, 2, 4]), ALU.mult).then_inc(S["gate_step"], 1)
                dve.tensor_copy(xrow[par][:, :, DM + 4:DM + 5], tokno[:, :].unsqueeze(2)).then_inc(S["gate_step"], 1)
                dve.wait_ge(S["gate_step"], g0 + 5)
                dve.tensor_scalar(tokno[:, :], tokno[:, :], 256.0, None, ALU.add).then_inc(S["tok_step"], 1)
                dve.wait_ge(S["tok_step"], c + 1)

            def step(i, par, front, att, back, route):
                f, a, b = i + 1, i, i - 1
                if front:
                    dve.wait_ge(S["e_done"], f + 1)
                    wait(dve, S["yg_ready"], 2 * f)
                    dve.tensor_tensor(y[:, :, :], M0[:, :].rearrange("p (u n) -> p u n", u=2),
                                      vec[:, 0:1, :].to_broadcast([128, 2, DM]), ALU.add).then_inc(S["y_ready"], 1)
                    stats(lambda u: y[:, u, :], st1, mv1, f, "st1_ready", "mv1_ready", S["y_ready"], f + 1)
                if isinstance(i, int) and i < 0:
                    dve.wait_ge(S["const_in"], 16 * 4)
                    dve.tensor_scalar(wqkv[:, :, 0:DM], wqkv[:, :, 0:DM], -2.0, None, ALU.mult).then_inc(S["init_ready"], 1)
                    dve.wait_ge(S["init_ready"], 6)
                if back:
                    normalise(b, 0)
                    normalise(b, 1)
                if front:
                    inverse(sd1, rs1, f, "sd1_ready", "rs1_ready")
                    wait(dve, S["h_ready"], 2 * f)
                    if back:
                        dve.wait_ge(S["held_in"], 16 * i)
                    for u in range(2):
                        dve.scalar_tensor_tensor(yg[:, u, :], y[:, u, :], mv1[:, u, 0:1], vec[:, 1, :], ALU.subtract,
                                                 ALU.mult).then_inc(S["yg_ready"], 1)
                    for u in range(2):
                        dve.wait_ge(S["yg_ready"], 2 * f + u + 1)
                        dve.scalar_tensor_tensor(h[1 - par][:, u, :], yg[:, u, :], rs1[:, u:u + 1], vec[:, 2, :],
                                                 ALU.mult, ALU.add).then_inc(S["h_ready"], 1)
                if route:
                    gates(i - 2, par)
                if front:
                    stats(lambda u: h[1 - par][:, u, :], st2, mv2, f, "st2_ready", "mv2_ready", S["h_ready"], 2 * f + 2)
                if att:
                    densities(a, 0)
                if front:
                    inverse(sd2, rs2, f, "sd2_ready", "rs2_ready")
                    wait(dve, S["ht_done"], f)
                    for u in range(2):
                        dve.tensor_scalar(hn[:, u, :], h[1 - par][:, u, :], mv2[:, u, 0:1], rs2[:, u:u + 1],
                                          ALU.subtract, ALU.mult).then_inc(S["hn_ready"], 1)
                if back:
                    dve.wait_ge(S["wo_done"], i)
                    wait(dve, S["out_stored"], 16 * (i - 1))
                    dve.wait_ge(S["held_in"], 16 * i)
                    dve.tensor_tensor(x2[:, :, :], M2[:, :].rearrange("p (u n) -> p u n", u=2), held[:, :, :],
                                      ALU.add).then_inc(S["x2_ready"], 1)
                    stats(lambda u: x2[:, u, :], st3, mv3, b, "st3_ready", "mv3_ready", S["x2_ready"], i)
                if att:
                    add_density(a, 0)
                if back:
                    inverse(sd3, rs3, b, "sd3_ready", "rs3_ready")
                    wait(dve, S["scat_hi"], 32 * (i - 2))
                    wait(dve, S["scat_lo"], 32 * (i - 2))
                    for u in range(2):
                        dve.tensor_scalar(xrow[1 - par][:, u, 0:DM], x2[:, u, :], mv3[:, u, 0:1], rs3[:, u:u + 1],
                                          ALU.subtract, ALU.mult).then_inc(S["xn_ready"], 1)
                if att:
                    densities(a, 1)
                    add_density(a, 1)
                if front:
                    for u in range(2):
                        dve.wait_ge(S["v_done"], 2 * f + u + 1)
                        for c in range(2):
                            own = slice(64 * c, 64 * c + 64)
                            dve.tensor_copy(v[1 - par][own, u, :, c, :, 0:HD],
                                            PS[own, 2 * u + 1, 0:DM].rearrange("p (j g e) -> p j g e", j=8, g=2))\
                               .then_inc(S["v_ready"], 1)
                        dve.wait_ge(S["sq_ready"], 2 * f + u + 1)
                        if u == 0:
                            wait(dve, S["xy_done"], f)
                        dve.tensor_reduce(nrm[:, u, :, :].rearrange("p a b -> p (a b)"),
                                          sq[:, u, :].rearrange("p (a e) -> p a e", e=HD), AX.X, ALU.add)\
                           .then_inc(S["nrm_ready"], 1)
                        dve.wait_ge(S["nrm_ready"], 2 * f + u + 1)
                        dve.tensor_scalar(nrm[:, u, 0, :], nrm[:, u, 0, :], 0.25, None, ALU.mult).then_inc(S["nq_ready"], 1)
                        dve.wait_ge(S["nq_ready"], 2 * f + u + 1)
                        nq = nrm[:, u, 0, :].unsqueeze(2).to_broadcast([128, HEADS, 2])
                        nk = nrm[:, u, 1, :].unsqueeze(2).to_broadcast([128, HEADS, 2])
                        clip = k("clip").unsqueeze(1).to_broadcast([128, HEADS, 2])
                        neg = k("negclip").unsqueeze(1).to_broadcast([128, HEADS, 2])
                        dve.tensor_tensor(aug[:, u, 0, :, :, HD], nq, clip, ALU.mult).then_inc(S["aug_ready"], 1)
                        dve.tensor_tensor(aug[:, u, 1, :, :, HD + 1], nk, clip, ALU.mult).then_inc(S["aug_ready"], 1)
                        dve.scalar_tensor_tensor(out=xb[:, u, u, :, :].rearrange("p c h -> p h c"), in0=nk, scalar=1.0,
                                                 in1=neg, op0=ALU.subtract, op1=ALU.mult).then_inc(S["aug_ready"], 1)
                        dve.scalar_tensor_tensor(out=yb[:, u, :, :].rearrange("p c h -> p h c"), in0=nq, scalar=1.0,
                                                 in1=neg, op0=ALU.subtract, op1=ALU.mult).then_inc(S["aug_ready"], 1)
                if back:
                    dve.wait_ge(S["lg_done"], i)
                    dve.tensor_tensor(lg[:, :, :], P1[:, 0:8].rearrange("p (u e) -> p u e", u=2),
                                      rbias[:, :].unsqueeze(1).to_broadcast([128, 2, 4]), ALU.add).then_inc(S["lg_ready"], 1)
                    dve.wait_ge(S["lg_ready"], i)
                    g0 = 4 * b
                    for u in range(2):
                        other = lg[:, u, :].unsqueeze(1).to_broadcast([128, 4, 4])
                        this = lg[:, u, :].unsqueeze(2).to_broadcast([128, 4, 4])
                        dve.tensor_tensor(gt[:, u, :, :], other, this, ALU.is_gt).then_inc(S["gt_ready"], 1)
                        dve.tensor_tensor(ge[:, u, :, :], other, this, ALU.is_ge).then_inc(S["ge_ready"], 1)
                    dve.tensor_reduce(m1[:, :, 0], lg[:, :, :], AX.X, ALU.max).then_inc(S["rk_ready"], 1)
                    dve.wait_ge(S["gt_ready"], 4 * b + 2)
                    dve.wait_ge(S["ge_ready"], 4 * b + 2)
                    dve.tensor_tensor(gt[:, :, :, :].rearrange("p u i j -> p u (i j)"),
                                      gt[:, :, :, :].rearrange("p u i j -> p u (i j)"),
                                      k("after").unsqueeze(1).to_broadcast([128, 2, 16]), ALU.mult).then_inc(S["gt_ready"], 1)
                    dve.tensor_tensor(ge[:, :, :, :].rearrange("p u i j -> p u (i j)"),
                                      ge[:, :, :, :].rearrange("p u i j -> p u (i j)"),
                                      k("before").unsqueeze(1).to_broadcast([128, 2, 16]), ALU.mult).then_inc(S["ge_ready"], 1)
                    dve.wait_ge(S["gt_ready"], 4 * b + 3)
                    dve.wait_ge(S["ge_ready"], 4 * b + 3)
                    dve.tensor_tensor(gt[:, :, :, :], gt[:, :, :, :], ge[:, :, :, :], ALU.add).then_inc(S["gt_ready"], 1)
                    dve.wait_ge(S["rk_ready"], 2 * b + 1)
                    wait(dve, S["ex_ready"], b)
                    dve.tensor_tensor(lm[:, :, :], lg[:, :, :], m1[:, :, :].to_broadcast([128, 2, 4]), ALU.subtract)\
                       .then_inc(S["lm_ready"], 1)
                    dve.wait_ge(S["gt_ready"], 4 * b + 4)
                    dve.tensor_reduce(rk[:, :, :].rearrange("p u e -> p (u e)"),
                                      gt[:, :, :, :].rearrange("p u i j -> p (u i) j"), AX.X, ALU.add)\
                       .then_inc(S["rk_ready"], 1)
                    dve.wait_ge(S["rk_ready"], 2 * b + 2)
                    wait(dve, S["slot_ready"], 2 * (i - 2))
                    dve.tensor_scalar(mask[1 - par][:, :, :], rk[:, :, :], 1.5, None, ALU.is_lt).then_inc(S["mask_ready"], 1)
                    dve.tensor_copy(ge[:, 0, 0, 0:1], k("one")).then_inc(S["ge_ready"], 1)
                    dve.wait_ge(S["ge_ready"], 4 * b + 4)
                if att:
                    probabilities(a, 0)
                if front:
                    dve.wait_ge(S["tk_done"], 2 * f + 1)
                    if att:
                        dve.wait_ge(S["d_done"], 2 * a + 2)
                    dve.tensor_copy(tk[:, 0, 4:8, :], M1[:, :].rearrange("p (m n) -> p m n", m=4))\
                       .then_inc(S["tkb_ready"], 1)
                if front:
                    dve.wait_ge(S["tk_done"], 2 * f + 2)
                    dve.tensor_copy(tk[:, 1, 4:8, :], M3[:, :].rearrange("p (m n) -> p m n", m=4))\
                       .then_inc(S["tkb_ready"], 1)
                    dve.wait_ge(S["xy_done"], f + 1)
                    if att:
                        dve.wait_ge(S["p_done"], 4 * a + 4)
                    dve.tensor_copy(xT[:, :, :], P0[0:64, 0:256].rearrange("p (u n) -> p u n", u=2))\
                       .then_inc(S["xt_ready"], 1)
                    dve.tensor_tensor(ybd[:, :].rearrange("p (h q) -> p h q", h=HEADS),
                                      P0[0:64, 256:320].unsqueeze(1).to_broadcast([64, HEADS, 64]),
                                      K[0:64, C["head"][0]:C["head"][1]].unsqueeze(2).to_broadcast([64, HEADS, 64]),
                                      ALU.mult).then_inc(S["ybd_ready"], 1)
                if att:
                    probabilities(a, 1)
            walk(dve, step)

            n = [0]

            def link(ins):
                n[0] += 1
                ins.then_inc(S["tab_step"], 1)
                dve.wait_ge(S["tab_step"], n[0])

            dve.wait_ge(S["slot_step"], SLOTTED * (PAIRS - 1) + BASED)
            link(dve.tensor_tensor(cnt[:, :], base[:, :], k("region"), ALU.subtract))
            link(dve.tensor_tensor(cmpb[:, :, :], cnt[:, :].unsqueeze(2).to_broadcast([128, 4, 9]),
                                   k("steps").unsqueeze(1).to_broadcast([128, 4, 9]), ALU.is_gt))
            link(dve.tensor_reduce(nb[:, :], cmpb[:, :, :], AX.X, ALU.add))
            link(dve.tensor_copy(cum[:, 0:1], nb[:, 0:1]))
            for e in range(1, 4):
                link(dve.tensor_tensor(cum[:, e:e + 1], cum[:, e - 1:e], nb[:, e:e + 1], ALU.add))
            link(dve.tensor_tensor(past[:, :, :], k("blockno").unsqueeze(1).to_broadcast([128, 4, BLOCKS]),
                                   cum[:, :].unsqueeze(2).to_broadcast([128, 4, BLOCKS]), ALU.is_ge))
            link(dve.tensor_tensor(be[:, :], past[:, 0, :], past[:, 1, :], ALU.add))
            link(dve.tensor_tensor(be[:, :], be[:, :], past[:, 2, :], ALU.add))
            link(dve.tensor_tensor(bs[:, :, :], past[:, 0:3, :], nb[:, 0:3].unsqueeze(2).to_broadcast([128, 3, BLOCKS]),
                                   ALU.mult))
            link(dve.tensor_tensor(bt1[:, :], k("blockno"), bs[:, 0, :], ALU.subtract))
            link(dve.tensor_tensor(bt1[:, :], bt1[:, :], bs[:, 1, :], ALU.subtract))
            link(dve.tensor_tensor(bt1[:, :], bt1[:, :], bs[:, 2, :], ALU.subtract))
            link(dve.tensor_scalar(bt1[:, :], bt1[:, :], float(BLOCK), None, ALU.mult))
            link(dve.tensor_scalar(bt2[:, :], be[:, :], float(REGION), None, ALU.mult))
            link(dve.tensor_tensor(brow[:, :], bt1[:, :], bt2[:, :], ALU.add))
            link(dve.tensor_scalar(bt1[:, :], brow[:, :], -1.0, float(EXPERTS * REGION), ALU.mult, ALU.add))
            link(dve.tensor_tensor(bt2[:, :], bt1[:, :], past[:, 3, :], ALU.mult))
            link(dve.tensor_tensor(tabf[:, BLOCKS:2 * BLOCKS], brow[:, :], bt2[:, :], ALU.add))
            link(dve.tensor_copy(tabf[:, 0:BLOCKS], be[:, :]))
            dve.tensor_copy(shared.table[:, :], tabf[0:1, :]).then_inc(S["tab_ready"], 1)
            link(dve.tensor_scalar(chosen[:, :, 0], past[:, 0, :], -1.0, 1.0, ALU.mult, ALU.add))
            for e in (1, 2):
                link(dve.tensor_tensor(chosen[:, :, e], past[:, e - 1, :], past[:, e, :], ALU.subtract))
            link(dve.tensor_copy(chosen[:, :, 3], past[:, 2, :]))

        @block.scalar
        def _(act):
            act.preload_act_table(ACT.Sqrt)
            act.wait_ge(S["embed_in"], 16 * 3)
            act.wait_ge(S["zero_ready"], 4)

            def deviation(mv, sd, p, eps, n1, n2, used):
                act.wait_ge(S[n1], 2 * p + 2)
                wait(act, S[used], p)
                act.activation(sd[:, :], mv[:, :, 1], ACT.Sqrt, bias=k(eps)).then_inc(S[n2], 1)

            def distances(a, u):
                act.wait_ge(S["d_done"], 2 * a + u + 1)
                for half in range(2):
                    if half == 0:
                        wait(act, S["w_ready"], 2 * a)
                    act.activation(dist[:, u, half * 512:(half + 1) * 512], DB[half][:, :], ACT.Relu)\
                       .then_inc(S["dist_ready"], 1)

            def roots(a, u):
                act.wait_ge(S["dsum_ready"], 2 * a + u + 1)
                act.activation(dist[:, u, :], dist[:, u, :], ACT.Sqrt).then_inc(S["ra_ready"], 1)
                act.activation(dsum[:, u, :], dsum[:, u, :], ACT.Sqrt).then_inc(S["rb_ready"], 1)

            def split(f, u):
                act.wait_ge(S["qk_done"], 2 * f + u + 1)
                wait(act, S["nrm_ready"], 2 * f + u - 1 if u else 2 * f)
                act.activation(sq[:, u, :], PS[:, 2 * u, :], ACT.Square).then_inc(S["sq_ready"], 1)
                if u == 0:
                    wait(act, S["tq_done"], 2 * f)
                for c in range(2):
                    own = slice(64 * c, 64 * c + 64)
                    act.activation(aug[own, u, :, :, c, 0:HD],
                                   PS[own, 2 * u, :].rearrange("p (a h e) -> p a h e", a=2, h=HEADS), ACT.Copy)\
                       .then_inc(S["data_ready"], 1)

            def weights(a, u):
                act.wait_ge(S["c_ready"], 2 * a + u + 1)
                act.activation(dist[:, u, :], dist[:, u, :], ACT.Ln).then_inc(S["ln_ready"], 1)
                act.wait_ge(S["ln_ready"], 2 * a + u + 1)
                act.activation(dist[:, u, :], dist[:, u, :], ACT.Exp, scale=-2.0).then_inc(S["e_ready"], 1)

            def factors(f, a, u, att):
                act.wait_ge(S["tk_done"], 2 * f + u + 1)
                if att and u == 0:
                    act.wait_ge(S["d_done"], 2 * a + 2)
                act.activation(tk[:, u, 0:4, :].rearrange("p a b -> p (a b)"), PS[:, 2 * u, :], ACT.Copy)\
                   .then_inc(S["tka_ready"], 1)
                act.wait_ge(S["tq_done"], 2 * f + u + 1)
                for g in range(2):
                    own = slice(64 * g, 64 * g + 64)
                    act.activation(tq[own, u, :, g, :], DB[u][own, :].rearrange("p (m q) -> p m q", m=8),
                                   ACT.Copy).then_inc(S["tq_ready"], 1)

            def step(i, par, front, att, back, route):
                f, a, b = i + 1, i, i - 1
                if front:
                    deviation(mv1, sd1, f, "eps_tok", "mv1_ready", "sd1_ready", "rs1_ready")
                if att:
                    distances(a, 0)
                if back:
                    act.wait_ge(S["at_done"], i)
                    wait(act, S["wo_done"], b)
                    for u in range(2):
                        act.activation(at[:, u, :, :, :].rearrange("p g c q -> p c g q"),
                                       M1[:, u * 256:(u + 1) * 256].rearrange("p (c g q) -> p c g q", c=2, g=2),
                                       ACT.Copy).then_inc(S["at_ready"], 1)
                if front:
                    deviation(mv2, sd2, f, "eps_ln", "mv2_ready", "sd2_ready", "rs2_ready")
                    act.wait_ge(S["ht_done"], f + 1)
                    wait(act, S["v_done"], 2 * f)
                    act.activation(hnT[:, :, :, :].rearrange("p a b c -> p (a b c)"), M3[:, :], ACT.Copy)\
                       .then_inc(S["hnT_ready"], 1)
                if att:
                    distances(a, 1)
                if back:
                    deviation(mv3, sd3, b, "eps_ln", "mv3_ready", "sd3_ready", "rs3_ready")
                if att:
                    roots(a, 0)
                if front:
                    split(f, 0)
                if back:
                    act.wait_ge(S["xnt_done"], i)
                    wait(act, S["lg_done"], b)
                    act.activation(xnT[:, :, :, :].rearrange("p a b c -> p (a b c)"), P1[:, :], ACT.Copy)\
                       .then_inc(S["xnT_ready"], 1)
                if att:
                    roots(a, 1)
                act.preload_act_table_set("natural_log_exp_and_others")
                if front:
                    split(f, 1)
                if att:
                    weights(a, 0)
                if front:
                    factors(f, a, 0, att)
                if att:
                    weights(a, 1)
                if back:
                    act.wait_ge(S["lm_ready"], i)
                    wait(act, S["gate_step"], 5 * b)
                    act.activation(ex[:, :, :], lm[:, :, :], ACT.Exp).then_inc(S["ex_ready"], 1)
                if front:
                    factors(f, a, 1, att)
                if back:
                    act.wait_ge(S["px_done"], i)
                    wait(act, S["slot_ready"], 2 * b)
                    act.activation(px[:, :, :, :].rearrange("p a b c -> p (a b c)"), P1[:, 16:32], ACT.Copy)\
                       .then_inc(S["px_ready"], 1)
            walk(act, step)

        @block.gpsimd
        def _(pool):
            pool.wait_ge(S["embed_in"], 16 * 3)
            pool.memset(pad[:, :, :], 0.0).then_inc(S["padzero_ready"], 1)
            for s in range(2):
                pool.memset(xrow[s][:, :, DM + 4:ROW], 0.0).then_inc(S["padzero_ready"], 1)
            pool.wait_ge(S["padzero_ready"], 3)
            pool.tensor_copy(pad[:, :, DM + 4:DM + 5], k("dump").unsqueeze(2)).then_inc(S["pad_ready"], 1)

            def step(i, par, front, att, back, route):
                f, a, b = i + 1, i, i - 1
                if route:
                    c = i - 2
                    s0 = SLOTTED * c
                    pool.wait_ge(S["mask_ready"], c + 1)

                    def link(n, ins):
                        ins.then_inc(S["slot_step"], 1)
                        pool.wait_ge(S["slot_step"], s0 + n)
                    link(1, pool.tensor_tensor(t2[:, :, 0:1], mask[par][:, :, 0:1], mask[par][:, :, 1:2], ALU.add))
                    link(2, pool.tensor_tensor(t2[:, :, 1:2], t2[:, :, 0:1], mask[par][:, :, 2:3], ALU.add))
                    pool.wait_ge(S["px_ready"], c + 1)
                    link(3, pool.tensor_tensor(slot[:, 0, :], px[:, 0, 0, :], base[:, :], ALU.add))
                    link(4, pool.tensor_tensor(mid[:, :], px[:, 1, 0, :], base[:, :], ALU.add))
                    link(5, pool.tensor_tensor(slot[:, 1, :], px[:, 0, 1, :], mid[:, :], ALU.add))
                    link(BASED, pool.tensor_tensor(base[:, :], px[:, 1, 1, :], mid[:, :], ALU.add))
                    if isinstance(c, int) and c == PAIRS - 2:
                        pool.tensor_copy(padrow[:, :], base[0:1, :]).then_inc(S["padrow_ready"], 1)
                        pool.wait_ge(S["padrow_ready"], 1)
                    link(7, pool.tensor_tensor(slot[:, :, :], slot[:, :, :], mask[par][:, :, :], ALU.mult))
                    link(8, pool.tensor_tensor(t3[:, :, 0:1], slot[:, :, 1:2], mask[par][:, :, 0:1], ALU.mult))
                    link(9, pool.tensor_tensor(t3[:, :, 1:3], slot[:, :, 2:4], t2[:, :, :], ALU.mult))
                    link(10, pool.tensor_tensor(hi[:, :, :], t3[:, :, 0:1], t3[:, :, 1:2], ALU.add))
                    link(11, pool.tensor_tensor(hi[:, :, :], hi[:, :, :], t3[:, :, 2:3], ALU.add))
                    link(12, pool.tensor_tensor(t2[:, :, :], slot[:, :, 0:2], slot[:, :, 2:4], ALU.add))
                    link(13, pool.tensor_tensor(tot[:, :, :], t2[:, :, 0:1], t2[:, :, 1:2], ALU.add))
                    link(SLOTTED, pool.tensor_tensor(lo[:, :, :], tot[:, :, :], hi[:, :, :], ALU.subtract))
                    wait(pool, S["scat_hi"], 32 * c)
                    wait_apart(pool, S["passed_pool"], S["scat_lo"], 32 * c)
                    pool.tensor_copy(ihi[:, :, :], hi[:, :, :]).then_inc(S["slot_ready"], 1)
                    pool.tensor_copy(ilo[:, :, :], lo[:, :, :]).then_inc(S["slot_ready"], 1)
                    pool.wait_ge(S["slot_ready"], 2 * c + 2)
                if route:
                    if isinstance(c, int) and c == PAIRS - 1:
                        pool.wait_ge(S["pad_out"], 16 * (2 * EXPERTS + 1))
                    wait_apart(pool, S["passed_pool"], S["gate_step"], 5 * c + 5)
                    for u in range(2):
                        for ix, done in ((ihi, "scat_hi"), (ilo, "scat_lo")):
                            pool.indirect_dma_start(rows[:, :], bass.IndirectOffsetOnAxis(ap=ix[:, u, :], axis=0),
                                                    xrow[par][:, u, :], None).then_inc(S[done], 16)
                if att:
                    for u in range(2):
                        pool.wait_ge(S["ra_ready"], 2 * a + u + 1)
                        pool.wait_ge(S["rb_ready"], 2 * a + u + 1)
                        pool.tensor_tensor(dist[:, u, :], dist[:, u, :], dsum[:, u, :], ALU.add)\
                            .then_inc(S["c_ready"], 1)
            walk(pool, step)


def mixture_phase(nc, rows, w13, w2, consts, out, shared):
    with ExitStack() as ctx:
        def sb(name, shape, dt=F32):
            return ctx.enter_context(nc.sbuf_tensor(name, shape, dt))

        def sem(name):
            return ctx.enter_context(nc.semaphore(name))

        ident = sb("identb", [128, 128])
        gate = sb("gate", [128, 4])
        gsel = sb("gsel", [128, 4, EXPERTS])
        gsum = sb("gsum", [128, 4, 2])
        tok = sb("tok", [128, 4, 1], U32)
        chosen, xg, wa, wb = shared.chosen, shared.xg, shared.wa, shared.wb
        wa_in, wb_in = shared.wa_in, shared.wb_in
        wah = sb("wah", [128, FCH, 2, KC, 128], F32R)
        wal = sb("wal", [128, FCH, 2, KC, 128], F32R)
        wbh = sb("wbh", [128, FCH, DM], F32R)
        wbl = sb("wbl", [128, FCH, DM], F32R)
        xh = [sb(f"xh{s}", [128, KC, BLOCK], F32R) for s in range(2)]
        xl = [sb(f"xl{s}", [128, KC, BLOCK], F32R) for s in range(2)]
        act1 = sb("act1", [128, 2, BLOCK])
        hid = sb("hid", [128, 2, BLOCK])
        hh = sb("hh", [128, 4, BLOCK], F32R)
        hl = sb("hl", [128, 4, BLOCK], F32R)
        oy = sb("oy", [128, 4, DM])
        PS = ctx.enter_context(nc.psum_tensor("PB", [128, 8, 512], F32))

        names = """ident_in gsel_ready gsum_ready gate_ready tok_ready t_done xh_ready xl_ready wah_ready wal_ready wbh_ready
            wbl_ready h1_done h3_done act1_ready hid_ready hh_ready hl_ready o_done oy_act oy_dve added passed_pool""".split()
        S = {n: sem(n) for n in names}
        S["x_in"] = shared.x_in
        block = ctx.enter_context(nc.Block())
        T, H1, H3, O = 0, 2, 4, 6
        LAST = BLOCKS - 1
        LAG = 2
        AHEAD = FCH - LAG - 1


        def walk_blocks(eng, body):
            body(0, 0, True, False)
            body(1, 1, False, False)
            with eng.Fori(0, (LAST - 2) // 2) as n:
                for s in range(2):
                    body(2 * n + 2 + s, s, False, False)
            body(LAST, LAST % 2, False, True)

        @block.sync
        def _(sp):
            sp.dma_start(ident[:, :], consts[:, 0:128]).then_inc(S["ident_in"], 16)
            sp.wait_ge(shared.scat_hi, 32 * PAIRS)
            sp.wait_ge(shared.scat_lo, 32 * PAIRS)
            shared.load_rows(sp, rows, 0)
            e = shared.expert(sp, 0)
            for c in range(FCH):
                if c >= EARLY:
                    shared.load_wa(sp, w13, e, c)
                shared.load_wb(sp, w2, e, c)

            def load_x(i):
                wait(sp, S["t_done"], i)
                wait(sp, S["tok_ready"], i)
                wait(sp, S["gsel_ready"], i)
                shared.load_rows(sp, rows, i)

            def load_wa(i, e, c):
                wait(sp, S["wah_ready"], FCH * (i - 1) + c + 1)
                wait(sp, S["wal_ready"], FCH * (i - 1) + c + 1)
                shared.load_wa(sp, w13, e, c)

            def load_wb(i, e, c):
                wait(sp, S["wbh_ready"], FCH * (i - 1) + c + 1)
                wait(sp, S["wbl_ready"], FCH * (i - 1) + c + 1)
                shared.load_wb(sp, w2, e, c)

            def expert(i):
                return shared.expert(sp, i)

            e = expert(1)
            for c in range(FCH):
                load_wa(1, e, c)
            for c in range(AHEAD):
                load_wb(1, e, c)

            def body(j, e1, e2):
                for c in range(FCH):
                    if e2 is not None:
                        load_wa(j + 2, e2, c)
                    if AHEAD + c < FCH:
                        load_wb(j + 1, e1, AHEAD + c)
                    elif e2 is not None:
                        load_wb(j + 2, e2, AHEAD + c - FCH)
                    if c == 3:
                        load_x(j + 1)
            with sp.Fori(0, LAST - 1) as j:
                body(j, expert(j + 1), expert(j + 2))
            body(LAST - 1, expert(LAST), None)

        @block.tensor
        def _(pe):
            pe.wait_ge(S["ident_in"], 16)

            def transpose_x(i):
                pe.wait_ge(S["x_in"], 16 * (i + 1))
                wait(pe, S["xh_ready"], KC * i)
                wait(pe, S["xl_ready"], KC * i)
                for c in range(KC):
                    for r in range(4):
                        mm = pe.transpose(PS[:, T + c, r * 128:(r + 1) * 128], xg[:, r, c * 128:(c + 1) * 128],
                                          ident[:, :])
                mm.then_inc(S["t_done"], 1)

            def hidden(i, par, c):
                n = FCH * i + c
                pe.wait_ge(S["wah_ready"], n + 1)
                pe.wait_ge(S["wal_ready"], n + 1)
                pe.wait_ge(S["xh_ready"], KC * (i + 1))
                pe.wait_ge(S["xl_ready"], KC * (i + 1))
                for w, (bank, used, done) in enumerate(((H1, "act1_ready", "h1_done"), (H3, "hid_ready", "h3_done"))):
                    wait(pe, S[used], n - 1)
                    for m in range(KC):
                        for t, (a, b) in enumerate(((wah, xh[par]), (wah, xl[par]), (wal, xh[par]))):
                            mm = pe.matmul(PS[:, bank + c % 2, :], a[:, c, w, m, :], b[:, m, :],
                                           start=(m == 0 and t == 0), stop=(m == KC - 1 and t == 2))
                    mm.then_inc(S[done], 1)

            def output(i, c):
                n = FCH * i + c
                pe.wait_ge(S["hh_ready"], n + 1)
                pe.wait_ge(S["hl_ready"], n + 1)
                pe.wait_ge(S["wbh_ready"], n + 1)
                pe.wait_ge(S["wbl_ready"], n + 1)
                if c == 0:
                    wait(pe, S["oy_act"], 2 * i)
                    wait(pe, S["oy_dve"], 2 * i)
                for r in range(4):
                    for t, (a, b) in enumerate(((hh, wbh), (hh, wbl), (hl, wbh))):
                        mm = pe.matmul(PS[:, O + r // 2, (r % 2) * DM:(r % 2 + 1) * DM],
                                       a[:, c % 4, r * 128:(r + 1) * 128], b[:, c, :],
                                       start=(c == 0 and t == 0 and r % 2 == 0), stop=(c == FCH - 1 and t == 2),
                                       skip_group_check=True)
                mm.then_inc(S["o_done"], 1)

            def body(i, par, first, last):
                for c in range(FCH):
                    hidden(i, par, c)
                    if c >= LAG:
                        output(i, c - LAG)
                    elif not first:
                        output(i - 1, c - LAG + FCH)
                    if c == 5 and not last:
                        transpose_x(i + 1)
            transpose_x(0)
            walk_blocks(pe, body)
            for c in range(FCH - LAG, FCH):
                output(LAST, c)

        def high(act, src, dst, ready):
            act.activation(dst, src, ACT.Copy).then_inc(S[ready], 1)

        def low(dve, src, hi, dst, ready):
            dve.tensor_tensor(dst, src, hi.bitcast(F32), ALU.subtract).then_inc(S[ready], 1)

        @block.scalar
        def _(act):
            def split_a(i, c):
                act.wait_ge(wa_in[c], 16 * (i + 1))
                wait(act, S["h3_done"], FCH * (i - 1) + c + 1)
                high(act, wa[:, c, :, :, :].rearrange("p b c d -> p (b c d)"),
                     wah[:, c, :, :, :].rearrange("p b c d -> p (b c d)"), "wah_ready")

            def split_b(i, c):
                act.wait_ge(wb_in[c], 16 * (i + 1))
                wait(act, S["o_done"], FCH * (i - 1) + c + 1)
                high(act, wb[:, c, :], wbh[:, c, :], "wbh_ready")

            def split_x(i, par):
                act.wait_ge(S["t_done"], i + 1)
                wait(act, S["h3_done"], FCH * (i - 1))
                for c in range(KC):
                    high(act, PS[:, T + c, :], xh[par][:, c, :], "xh_ready")

            def rows_out(i):
                act.wait_ge(S["o_done"], FCH * (i + 1))
                act.wait_ge(S["gate_ready"], i + 1)
                wait(act, S["added"], 64 * i)
                for r in range(2):
                    act.activation(oy[:, r, :], PS[:, O, r * DM:(r + 1) * DM], ACT.Copy, scale=gate[:, r:r + 1])\
                       .then_inc(S["oy_act"], 1)

            def body(i, par, first, last):
                for c in range(FCH):
                    n = FCH * i + c
                    act.wait_ge(S["h1_done"], n + 1)
                    wait(act, S["hid_ready"], n - 1)
                    act.activation(act1[:, c % 2, :], PS[:, H1 + c % 2, :], ACT.Silu).then_inc(S["act1_ready"], 1)
                    act.wait_ge(S["hid_ready"], n + 1)
                    wait(act, S["o_done"], n - 3)
                    high(act, hid[:, c % 2, :], hh[:, c % 4, :], "hh_ready")
                    if c == LAG - 1 and not first:
                        rows_out(i - 1)
                    if c == 6 and not last:
                        split_x(i + 1, 1 - par)
                    if not last:
                        split_a(i + 1, c)
                    if AHEAD + c < FCH:
                        split_b(i, AHEAD + c)
                    elif not last:
                        split_b(i + 1, AHEAD + c - FCH)
            act.preload_act_table(ACT.Silu)
            for c in range(EARLY):
                split_a(0, c)
            split_x(0, 0)
            for c in range(EARLY, FCH):
                split_a(0, c)
            for c in range(AHEAD):
                split_b(0, c)
            walk_blocks(act, body)
            rows_out(LAST)

        @block.vector
        def _(dve):
            def split_a(i, c):
                dve.wait_ge(S["wah_ready"], FCH * i + c + 1)
                wait(dve, S["h3_done"], FCH * (i - 1) + c + 1)
                low(dve, wa[:, c, :, :, :].rearrange("p b c d -> p (b c d)"),
                    wah[:, c, :, :, :].rearrange("p b c d -> p (b c d)"),
                    wal[:, c, :, :, :].rearrange("p b c d -> p (b c d)"), "wal_ready")

            def split_b(i, c):
                dve.wait_ge(S["wbh_ready"], FCH * i + c + 1)
                wait(dve, S["o_done"], FCH * (i - 1) + c + 1)
                low(dve, wb[:, c, :], wbh[:, c, :], wbl[:, c, :], "wbl_ready")

            def split_x(i, par):
                wait(dve, S["h3_done"], FCH * (i - 1))
                for c in range(KC):
                    dve.wait_ge(S["xh_ready"], KC * i + c + 1)
                    low(dve, PS[:, T + c, :], xh[par][:, c, :], xl[par][:, c, :], "xl_ready")

            def rows_out(i):
                dve.wait_ge(S["o_done"], FCH * (i + 1))
                dve.wait_ge(S["gate_ready"], i + 1)
                wait(dve, S["added"], 64 * i)
                for r in range(2, 4):
                    dve.tensor_scalar(oy[:, r, :], PS[:, O + 1, (r - 2) * DM:(r - 1) * DM], gate[:, r:r + 1], None,
                                      ALU.mult).then_inc(S["oy_dve"], 1)

            def body(i, par, first, last):
                for c in range(FCH):
                    n = FCH * i + c
                    dve.wait_ge(S["act1_ready"], n + 1)
                    dve.wait_ge(S["h3_done"], n + 1)
                    wait(dve, S["hh_ready"], n - 1)
                    dve.tensor_tensor(hid[:, c % 2, :], PS[:, H3 + c % 2, :], act1[:, c % 2, :], ALU.mult)\
                       .then_inc(S["hid_ready"], 1)
                    dve.wait_ge(S["hh_ready"], n + 1)
                    wait(dve, S["o_done"], n - 3)
                    low(dve, hid[:, c % 2, :], hh[:, c % 4, :], hl[:, c % 4, :], "hl_ready")
                    if c == LAG - 1 and not first:
                        rows_out(i - 1)
                    if c == 6 and not last:
                        split_x(i + 1, 1 - par)
                    if not last:
                        split_a(i + 1, c)
                    if AHEAD + c < FCH:
                        split_b(i, AHEAD + c)
                    elif not last:
                        split_b(i + 1, AHEAD + c - FCH)
            for c in range(EARLY):
                split_a(0, c)
            split_x(0, 0)
            for c in range(EARLY, FCH):
                split_a(0, c)
            for c in range(AHEAD):
                split_b(0, c)
            walk_blocks(dve, body)
            rows_out(LAST)

        @block.gpsimd
        def _(pool):
            def body(i):
                wait_apart(pool, S["passed_pool"], S["x_in"], 16 * (i + 1))
                pool.tensor_copy(tok[:, :, :], xg[:, :, DM + EXPERTS:DM + EXPERTS + 1]).then_inc(S["tok_ready"], 1)
                pool.tensor_tensor(gsel[:, :, :], xg[:, :, DM:DM + EXPERTS],
                                   chosen[:, bass.ds(i, 1), :].to_broadcast([128, 4, EXPERTS]), ALU.mult)\
                    .then_inc(S["gsel_ready"], 1)
                pool.wait_ge(S["gsel_ready"], i + 1)
                pool.tensor_tensor(gsum[:, :, :], gsel[:, :, 0:2], gsel[:, :, 2:4], ALU.add).then_inc(S["gsum_ready"], 1)
                pool.wait_ge(S["gsum_ready"], i + 1)
                pool.tensor_tensor(gate[:, :].unsqueeze(2), gsum[:, :, 0:1], gsum[:, :, 1:2], ALU.add)\
                    .then_inc(S["gate_ready"], 1)
                pool.wait_ge(S["tok_ready"], i + 1)
                pool.wait_ge(S["oy_act"], 2 * (i + 1))
                wait_apart(pool, S["passed_pool"], S["oy_dve"], 2 * (i + 1))
                for t in range(4):
                    pool.indirect_dma_start(out[:, :], bass.IndirectOffsetOnAxis(ap=tok[:, t, :], axis=0),
                                            oy[:, t, :], None, compute_op=ALU.add).then_inc(S["added"], 16)
                pool.wait_ge(S["added"], 64 * (i + 1))
            with pool.Fori(0, BLOCKS) as i:
                body(i)


def program(nc, patches, w_tok, vecs, w_qkv, w_o, w_r, w13, w2, consts, out):
    rows = nc.dram_tensor("rows", [EXPERTS * REGION + BLOCK, ROW], F32).ap()
    with ExitStack() as ctx:
        shared = Shared(nc, ctx)
        attention_phase(nc, patches, w_tok, vecs, w_qkv, w_o, w_r, consts, w13, w2, out, rows, shared)
        mixture_phase(nc, rows, w13, w2, consts, out, shared)


def layout(x, L0_tok_W, L0_tok_b, L0_tok_gamma, L0_tok_beta, L0_attn_Wq, L0_attn_Wk, L0_attn_Wv, L0_attn_Wo,
           L0_ffn_router_w, L0_ffn_router_b, L0_ffn_w1, L0_ffn_w3, L0_ffn_w2):
    import numpy as np

    padded = np.zeros((CLIPS, 128, 128), np.float32)
    padded[:, :x.shape[1], :] = x
    p = padded.reshape(PAIRS, 2, 2, 8, 16, 8, 16).transpose(0, 4, 6, 1, 2, 3, 5).reshape(PAIRS, KC, 128, 2, 128)

    def chunks(w):
        return np.ascontiguousarray(w.reshape(w.shape[0] // 128, 128, -1).transpose(1, 0, 2))

    qkv = np.concatenate([L0_attn_Wq.T, L0_attn_Wk.T, L0_attn_Wv.T], axis=1)
    wo = L0_attn_Wo.T.reshape(8, 2, HD, DM).transpose(0, 2, 1, 3).reshape(128, 2, DM)
    w13 = np.stack([L0_ffn_w1, L0_ffn_w3], axis=0).reshape(2, EXPERTS, KC, 128, FCH, 128)
    vecs = np.concatenate([L0_tok_b, L0_tok_gamma, L0_tok_beta, L0_ffn_router_b])
    return {
        "patches": np.ascontiguousarray(p.transpose(0, 2, 3, 1, 4)),
        "w_tok": chunks(L0_tok_W),
        "vecs": np.ascontiguousarray(np.broadcast_to(vecs, (128, vecs.size))),
        "w_qkv": chunks(qkv),
        "w_o": np.ascontiguousarray(wo),
        "w_r": chunks(L0_ffn_router_w),
        "w13": np.ascontiguousarray(w13.transpose(1, 4, 3, 0, 2, 5)).reshape(EXPERTS, FCH, 128, 4 * 128),
        "w2": np.ascontiguousarray(L0_ffn_w2).reshape(EXPERTS, FCH, 128, DM),
        "consts": constants(),
    }


OUT = (TOKENS + BLOCK, DM)


def kernel(**inputs):
    import numpy as np
    import concourse.bacc as bacc
    from concourse.bass_utils import run_bass_kernel_spmd

    nc = bacc.Bacc("TRN2", target_bir_lowering=False, num_devices=1)
    arrays = layout(**{n: np.asarray(a) for n, a in inputs.items()})
    args = {n: nc.dram_tensor(f"in_{n}", a.shape, mybir.dt.from_np(a.dtype), kind="ExternalInput").ap()
            for n, a in arrays.items()}
    result = nc.dram_tensor("result", OUT, F32, kind="ExternalOutput").ap()
    program(nc, out=result, **args)
    r = run_bass_kernel_spmd(nc, [{f"in_{n}": a for n, a in arrays.items()}], core_ids=[0])
    return r.results[0]["result"][:TOKENS].reshape(CLIPS, SEQ, DM)
```
